# Optimizing a Trainium2 kernel written in Bass

```python
import numpy as np
import jax
import jax.numpy as jnp

def _softmax(x, axis=-1):
    return jax.nn.softmax(x, axis=axis)

def _gelu(x):
    return jax.nn.gelu(x, approximate=True)

def _silu(x):
    return jax.nn.silu(x)

def _sigmoid(x):
    return jax.nn.sigmoid(x)

def _layernorm(x, axis=-1, eps=1e-05):
    m = jnp.mean(x, axis=axis, keepdims=True)
    v = jnp.var(x, axis=axis, keepdims=True)
    return (x - m) / jnp.sqrt(v + eps)

def _scatter_add(tgt, idx, src, axis=0):
    return tgt.at[idx].add(src)

def _segment_sum(src, seg, n):
    return jax.ops.segment_sum(src, seg, n)
kernel_name = 'mk_dlrm_tower_d1_rec_r8_637d7f'

def setup_inputs(seed: int=0):
    np.random.seed(seed)
    _w = jnp.asarray

    def _rec_inputs():
        import jax
        import jax.numpy as jnp
        _tk = jax.random.key(seed)
        dense_ctx = jax.random.normal(jax.random.fold_in(_tk, 190), (512, 16), jnp.float32)
        ids = jnp.stack([jax.random.randint(jax.random.fold_in(_tk, 200 + f), (512,), 0, v, jnp.int32) for f, v in enumerate([1250, 1000, 1000, 1250, 12500, 12500, 1250, 125000, 1000, 12500, 1250, 1250, 1000, 1250, 12500, 1000, 12500, 1000, 1000, 1250, 1250, 12500, 1000, 1000, 1250, 1000, 12500])], axis=1)
        tbl_0 = 0.05 * jax.random.normal(jax.random.fold_in(_tk, 500 + 0), (1250, 128), jnp.float32)
        tbl_1 = 0.05 * jax.random.normal(jax.random.fold_in(_tk, 500 + 1), (1000, 128), jnp.float32)
        tbl_2 = 0.05 * jax.random.normal(jax.random.fold_in(_tk, 500 + 2), (1000, 128), jnp.float32)
        tbl_3 = 0.05 * jax.random.normal(jax.random.fold_in(_tk, 500 + 3), (1250, 128), jnp.float32)
        tbl_4 = 0.05 * jax.random.normal(jax.random.fold_in(_tk, 500 + 4), (12500, 128), jnp.float32)
        tbl_5 = 0.05 * jax.random.normal(jax.random.fold_in(_tk, 500 + 5), (12500, 128), jnp.float32)
        tbl_6 = 0.05 * jax.random.normal(jax.random.fold_in(_tk, 500 + 6), (1250, 128), jnp.float32)
        tbl_7 = 0.05 * jax.random.normal(jax.random.fold_in(_tk, 500 + 7), (125000, 128), jnp.float32)
        tbl_8 = 0.05 * jax.random.normal(jax.random.fold_in(_tk, 500 + 8), (1000, 128), jnp.float32)
        tbl_9 = 0.05 * jax.random.normal(jax.random.fold_in(_tk, 500 + 9), (12500, 128), jnp.float32)
        tbl_10 = 0.05 * jax.random.normal(jax.random.fold_in(_tk, 500 + 10), (1250, 128), jnp.float32)
        tbl_11 = 0.05 * jax.random.normal(jax.random.fold_in(_tk, 500 + 11), (1250, 128), jnp.float32)
        tbl_12 = 0.05 * jax.random.normal(jax.random.fold_in(_tk, 500 + 12), (1000, 128), jnp.float32)
        tbl_13 = 0.05 * jax.random.normal(jax.random.fold_in(_tk, 500 + 13), (1250, 128), jnp.float32)
        tbl_14 = 0.05 * jax.random.normal(jax.random.fold_in(_tk, 500 + 14), (12500, 128), jnp.float32)
        tbl_15 = 0.05 * jax.random.normal(jax.random.fold_in(_tk, 500 + 15), (1000, 128), jnp.float32)
        tbl_16 = 0.05 * jax.random.normal(jax.random.fold_in(_tk, 500 + 16), (12500, 128), jnp.float32)
        tbl_17 = 0.05 * jax.random.normal(jax.random.fold_in(_tk, 500 + 17), (1000, 128), jnp.float32)
        tbl_18 = 0.05 * jax.random.normal(jax.random.fold_in(_tk, 500 + 18), (1000, 128), jnp.float32)
        tbl_19 = 0.05 * jax.random.normal(jax.random.fold_in(_tk, 500 + 19), (1250, 128), jnp.float32)
        tbl_20 = 0.05 * jax.random.normal(jax.random.fold_in(_tk, 500 + 20), (1250, 128), jnp.float32)
        tbl_21 = 0.05 * jax.random.normal(jax.random.fold_in(_tk, 500 + 21), (12500, 128), jnp.float32)
        tbl_22 = 0.05 * jax.random.normal(jax.random.fold_in(_tk, 500 + 22), (1000, 128), jnp.float32)
        tbl_23 = 0.05 * jax.random.normal(jax.random.fold_in(_tk, 500 + 23), (1000, 128), jnp.float32)
        tbl_24 = 0.05 * jax.random.normal(jax.random.fold_in(_tk, 500 + 24), (1250, 128), jnp.float32)
        tbl_25 = 0.05 * jax.random.normal(jax.random.fold_in(_tk, 500 + 25), (1000, 128), jnp.float32)
        tbl_26 = 0.05 * jax.random.normal(jax.random.fold_in(_tk, 500 + 26), (12500, 128), jnp.float32)
        _rk = jax.random.fold_in(_tk, 7)
        W_top1 = 0.0521996 * jax.random.normal(jax.random.fold_in(_tk, 801), (367, 512), jnp.float32)
        W_top2 = 0.0441942 * jax.random.normal(jax.random.fold_in(_tk, 802), (512, 256), jnp.float32)
        W_top3 = 0.0625 * jax.random.normal(jax.random.fold_in(_tk, 803), (256, 1), jnp.float32)
        b_top1 = jnp.zeros((512,), jnp.float32)
        b_top2 = jnp.zeros((256,), jnp.float32)
        return (dense_ctx, ids, tbl_0, tbl_1, tbl_2, tbl_3, tbl_4, tbl_5, tbl_6, tbl_7, tbl_8, tbl_9, tbl_10, tbl_11, tbl_12, tbl_13, tbl_14, tbl_15, tbl_16, tbl_17, tbl_18, tbl_19, tbl_20, tbl_21, tbl_22, tbl_23, tbl_24, tbl_25, tbl_26, W_top1, b_top1, W_top2, b_top2, W_top3)
    dense_ctx, ids, tbl_0, tbl_1, tbl_2, tbl_3, tbl_4, tbl_5, tbl_6, tbl_7, tbl_8, tbl_9, tbl_10, tbl_11, tbl_12, tbl_13, tbl_14, tbl_15, tbl_16, tbl_17, tbl_18, tbl_19, tbl_20, tbl_21, tbl_22, tbl_23, tbl_24, tbl_25, tbl_26, W_top1, b_top1, W_top2, b_top2, W_top3 = _rec_inputs()

    def _L0_rec_setup():
        import jax, jax.numpy as jnp
        import numpy as np
        key = jax.random.key(seed)
        B, F, D = (2048, 27, 128)
        inputs = jax.random.normal(key, (B, F, D), dtype=jnp.float32)
        return {'inputs': inputs, 'num_feas': F}
    _L0_rec_all = _L0_rec_setup()
    _L0_rec_in = {k: v for k, v in _L0_rec_all.items() if k in ()}
    del _L0_rec_all
    return {'dense_ctx': dense_ctx, 'ids': ids, 'tbl_0': tbl_0, 'tbl_1': tbl_1, 'tbl_2': tbl_2, 'tbl_3': tbl_3, 'tbl_4': tbl_4, 'tbl_5': tbl_5, 'tbl_6': tbl_6, 'tbl_7': tbl_7, 'tbl_8': tbl_8, 'tbl_9': tbl_9, 'tbl_10': tbl_10, 'tbl_11': tbl_11, 'tbl_12': tbl_12, 'tbl_13': tbl_13, 'tbl_14': tbl_14, 'tbl_15': tbl_15, 'tbl_16': tbl_16, 'tbl_17': tbl_17, 'tbl_18': tbl_18, 'tbl_19': tbl_19, 'tbl_20': tbl_20, 'tbl_21': tbl_21, 'tbl_22': tbl_22, 'tbl_23': tbl_23, 'tbl_24': tbl_24, 'tbl_25': tbl_25, 'tbl_26': tbl_26, 'W_top1': W_top1, 'b_top1': b_top1, 'W_top2': W_top2, 'b_top2': b_top2, 'W_top3': W_top3}

def reference(dense_ctx, ids, tbl_0, tbl_1, tbl_2, tbl_3, tbl_4, tbl_5, tbl_6, tbl_7, tbl_8, tbl_9, tbl_10, tbl_11, tbl_12, tbl_13, tbl_14, tbl_15, tbl_16, tbl_17, tbl_18, tbl_19, tbl_20, tbl_21, tbl_22, tbl_23, tbl_24, tbl_25, tbl_26, W_top1, b_top1, W_top2, b_top2, W_top3):
    import jax
    import jax.numpy as jnp

    def _L0_rec_ref(inputs, num_feas):
        import jax, jax.numpy as jnp
        import numpy as np
        dot_products = jnp.einsum('bnd,bmd->bnm', inputs, inputs)
        r, c = np.tril_indices(num_feas, k=-1)
        flat_interactions = dot_products[:, c, r]
        return flat_interactions
    e = jnp.stack([tbl_0[ids[:, 0]], tbl_1[ids[:, 1]], tbl_2[ids[:, 2]], tbl_3[ids[:, 3]], tbl_4[ids[:, 4]], tbl_5[ids[:, 5]], tbl_6[ids[:, 6]], tbl_7[ids[:, 7]], tbl_8[ids[:, 8]], tbl_9[ids[:, 9]], tbl_10[ids[:, 10]], tbl_11[ids[:, 11]], tbl_12[ids[:, 12]], tbl_13[ids[:, 13]], tbl_14[ids[:, 14]], tbl_15[ids[:, 15]], tbl_16[ids[:, 16]], tbl_17[ids[:, 17]], tbl_18[ids[:, 18]], tbl_19[ids[:, 19]], tbl_20[ids[:, 20]], tbl_21[ids[:, 21]], tbl_22[ids[:, 22]], tbl_23[ids[:, 23]], tbl_24[ids[:, 24]], tbl_25[ids[:, 25]], tbl_26[ids[:, 26]]], axis=1)
    z = _L0_rec_ref(e, 27)
    z = z.reshape(z.shape[0], -1)
    h = jnp.concatenate([z, dense_ctx], axis=1)
    h = jnp.maximum(h @ W_top1 + b_top1, 0.0)
    h = jnp.maximum(h @ W_top2 + b_top2, 0.0)
    y = h @ W_top3
    return y

_drawn_inputs = setup_inputs


def setup_inputs(seed=0):
    import zlib

    import numpy as np

    out = dict(_drawn_inputs(seed))
    spreads = {'b_top1': (0.0, 0.1), 'b_top2': (0.0, 0.1)}
    factors = {}
    for name, (base, spread) in spreads.items():
        noise = np.random.default_rng([zlib.crc32(name.encode()), seed]).standard_normal(out[name].shape)
        drawn = base * np.exp(spread * noise) if base else spread * noise
        out[name] = jnp.asarray(drawn.astype(out[name].dtype))
    for name, factor in factors.items():
        out[name] = (out[name] * factor).astype(out[name].dtype)
    return out
```

```python
from contextlib import ExitStack

import concourse.bass as bass
from concourse import mybir

F32 = mybir.dt.float32
I32 = mybir.dt.int32
ALU = mybir.AluOpType
ACT = mybir.ActivationFunctionType

B, F, D = 512, 27, 128
DENSE, H1, H2 = 16, 512, 256
P = 128
TILES = B // P
STRIPS, STRIP = 4, 32
HALF = STRIP // 2
STEPS = (F - 1) // 2
PAIRS = F * STEPS
BLOCKS = -(-(PAIRS + DENSE) // P)
PAIRS_IN = [min(P, PAIRS - c * P) for c in range(BLOCKS)]
K_IN = [min(P, PAIRS + DENSE - c * P) for c in range(BLOCKS)]
DENSE_AT = PAIRS_IN[-1]
EARLY = P // STEPS + 1
BANK = 512
PER_BANK = BANK // P
GROUPS = [list(range(f, min(f + PER_BANK, F))) for f in range(0, F, PER_BANK)]
NG = len(GROUPS)
TURN_BANKS = 3
M1, M2 = H1 // P, H2 // P


def on_vector(g):
    return g % 2 == 1


def build(nc, ids, tables, w1, w2, small, denseT, out):
    ctx = ExitStack()
    with ctx:
        def sb(name, shape, dt=F32):
            return ctx.enter_context(nc.sbuf_tensor(name, shape, dt))

        def pb(name, shape):
            return ctx.enter_context(nc.psum_tensor(name, shape, F32))

        def sem(name):
            return ctx.enter_context(nc.semaphore(name))

        ids_sb = sb("ids_sb", [P, TILES * F], I32)
        rows = sb("rows", [P, F, D])
        rowsT = sb("rowsT", [P, P * F + STRIP - F])
        rowsT_bf = rowsT[:, 0:P * F].rearrange("p (b f) -> p f b", f=F)
        gram = sb("gram", [P, F + STEPS, STRIP])
        pairs = sb("pairs", [P, F, STEPS])
        pairs_flat = pairs[:, :, :].rearrange("p a k -> p (a k)")
        zT = sb("zT", [P, BLOCKS, B])
        w1_sb = sb("w1_sb", [P, BLOCKS, H1])
        w2_sb = sb("w2_sb", [P, M1, H2])
        small_sb = sb("small_sb", [P, M1 + M2 + M2])
        b1_sb, b2_sb, w3_sb = small_sb[:, 0:M1], small_sb[:, M1:M1 + M2], small_sb[:, M1 + M2:]
        h1T = sb("h1T", [P, M1, P])
        h2T = sb("h2T", [P, M2, P])
        y_sb = sb("y_sb", [1, B])
        ident = sb("ident", [P, P])

        turn_ps = pb("turn_ps", [P, TURN_BANKS, BANK])
        gram_ps = pb("gram_ps", [P, 2, BANK])
        pair_ps = pb("pair_ps", [P, BANK])
        h1_ps = pb("h1_ps", [P, BANK])
        h2_ps = pb("h2_ps", [P, BANK])
        y_ps = h2_ps[0:1, M2 * P:M2 * P + P]

        ids_in = sem("ids_in")
        w1_in = [sem(f"w1_in{c}") for c in range(BLOCKS)]
        w2_in = sem("w2_in")
        small_in = sem("small_in")
        dense_in = sem("dense_in")
        ident_zero = sem("ident_zero")
        ident_ready = sem("ident_ready")
        pad_ready = sem("pad_ready")
        row_in = [sem(f"row_in{f}") for f in range(F)]
        turned = sem("turned")
        taken_v = sem("taken_v")
        taken_s = sem("taken_s")
        products = sem("products")
        regrouped = sem("regrouped")
        repeated = sem("repeated")
        early_ready = sem("early_ready")
        late_ready = sem("late_ready")
        paired = sem("paired")
        z_ready = sem("z_ready")
        l1_done = sem("l1_done")
        h1_ready = sem("h1_ready")
        l2_done = sem("l2_done")
        h2_ready = sem("h2_ready")
        l3_done = sem("l3_done")
        y_ready = sem("y_ready")
        out_done = sem("out_done")

        NV = sum(on_vector(g) for g in range(NG))
        NS = NG - NV

        def taken(t, g):
            v = sum(on_vector(x) for x in range(g))
            return (taken_v, t * NV + v + 1) if on_vector(g) else (taken_s, t * NS + g - v + 1)

        def window(a0, a1):
            flat = gram[:, :, :].rearrange("p j i -> p (j i)")
            start = flat[:, (a0 + 1) * STRIP + a0:]
            return bass.AP(start.tensor, start.offset,
                           [list(start.ap[0]), [STRIP + 1, a1 - a0], [STRIP, STEPS]])

        block = ctx.enter_context(nc.Block())

        @block.sync
        def _(sp):
            sp.dma_start(ids_sb[:, :], ids).then_inc(ids_in, 16)
            sp.dma_start(small_sb[:, :], small).then_inc(small_in, 16)
            for c in range(BLOCKS):
                sp.dma_start(w1_sb[0:K_IN[c], c, :], w1[c * P:c * P + K_IN[c], :]).then_inc(w1_in[c], 16)
            sp.dma_start(zT[DENSE_AT:DENSE_AT + DENSE, BLOCKS - 1, :], denseT).then_inc(dense_in, 16)
            sp.dma_start(w2_sb[:, :, :], w2.rearrange("(m p) n -> p m n", p=P)).then_inc(w2_in, 16)
            sp.wait_ge(y_ready, TILES)
            sp.dma_start(out, y_sb[:, :]).then_inc(out_done, 16)
            sp.wait_ge(out_done, 16)

        @block.gpsimd
        def _(pool):
            nc.gpsimd.memset(ident[:, :], 0.0).then_inc(ident_zero, 1)
            pool.wait_ge(ident_zero, 1)
            nc.gpsimd.affine_select(out=ident[:, :], in_=ident[:, :], compare_op=ALU.not_equal, fill=1.0,
                                    base=0, pattern=[[-1, P]], channel_multiplier=1).then_inc(ident_ready, 1)
            pool.wait_ge(ids_in, 16)
            for t in range(TILES):
                for f in range(F):
                    if t >= 1 and (f % PER_BANK == 0):
                        pool.wait_ge(turned, NG * (t - 1) + f // PER_BANK + 1)
                    nc.gpsimd.indirect_dma_start(
                        out=rows[:, f, :], out_offset=None, in_=tables[f],
                        in_offset=bass.IndirectOffsetOnAxis(ap=ids_sb[:, t * F + f:t * F + f + 1], axis=0),
                    ).then_inc(row_in[f], 16)

        @block.tensor
        def _(pe):
            pe.wait_ge(ident_ready, 1)
            pe.wait_ge(pad_ready, 1)
            with pe.Fori(0, TILES) as t:
                for g, features in enumerate(GROUPS):
                    if g >= TURN_BANKS:
                        pe.wait_ge(*taken(t, g - TURN_BANKS))
                    for n, f in enumerate(features):
                        pe.wait_ge(row_in[f], t * 16 + 16)
                        last = nc.tensor.transpose(turn_ps[:, g % TURN_BANKS, n * P:(n + 1) * P],
                                                   rows[:, f, :], ident[:, :])
                    last.then_inc(turned, 1)

                pe.wait_ge(taken_v, t * NV + NV)
                pe.wait_ge(taken_s, t * NS + NS)
                for i in range(STRIP):
                    for s in range(STRIPS):
                        at = (s * STRIP + i) * F
                        last = nc.tensor.matmul(
                            gram_ps[s * STRIP:(s + 1) * STRIP, i // HALF, (i % HALF) * F:(i % HALF + 1) * F],
                            rowsT[:, at:at + STRIP], rowsT[:, at:at + F], start=True, stop=True)
                last.then_inc(products, 1)

                pe.wait_ge(early_ready, t + 1)
                for c in range(BLOCKS):
                    if c == 1:
                        pe.wait_ge(late_ready, t + 1)
                    last = nc.tensor.transpose(pair_ps[0:PAIRS_IN[c], c * P:(c + 1) * P],
                                               pairs_flat[:, c * P:c * P + PAIRS_IN[c]], ident[:, :])
                last.then_inc(paired, 1)

                pe.wait_ge(z_ready, t + 1)
                for c in range(BLOCKS):
                    pe.wait_ge(w1_in[c], 16)
                pe.wait_ge(dense_in, 16)
                for m in range(M1):
                    for c in range(BLOCKS):
                        last = nc.tensor.matmul(h1_ps[:, m * P:(m + 1) * P],
                                                w1_sb[0:K_IN[c], c, m * P:(m + 1) * P],
                                                zT[0:K_IN[c], c, bass.ds(t * P, P)],
                                                start=c == 0, stop=c == BLOCKS - 1)
                last.then_inc(l1_done, 1)

                pe.wait_ge(h1_ready, t + 1)
                pe.wait_ge(w2_in, 16)
                for m in range(M2):
                    for c in range(M1):
                        last = nc.tensor.matmul(h2_ps[:, m * P:(m + 1) * P], w2_sb[:, c, m * P:(m + 1) * P],
                                                h1T[:, c, :], start=c == 0, stop=c == M1 - 1)
                last.then_inc(l2_done, 1)

                pe.wait_ge(h2_ready, t + 1)
                for c in range(M2):
                    last = nc.tensor.matmul(y_ps, w3_sb[:, c:c + 1], h2T[:, c, :],
                                            start=c == 0, stop=c == M2 - 1)
                last.then_inc(l3_done, 1)

        def group_out(g):
            n = len(GROUPS[g])
            src = turn_ps[:, g % TURN_BANKS, 0:n * P].rearrange("p (f b) -> p f b", f=n)
            return rowsT_bf[:, GROUPS[g][0]:GROUPS[g][0] + n, :], src

        @block.vector
        def _(dve):
            nc.vector.memset(rowsT[:, P * F:], 0.0).then_inc(pad_ready, 1)
            dve.wait_ge(small_in, 16)
            with dve.Fori(0, TILES) as t:
                for g in range(NG):
                    if on_vector(g):
                        dve.wait_ge(turned, t * NG + g + 1)
                        dst, src = group_out(g)
                        nc.vector.tensor_copy(dst, src).then_inc(taken_v, 1)

                dve.wait_ge(products, t + 1)
                nc.vector.transpose(gram[:, 0:F, :].rearrange("p j (h s) -> p j h s", h=2),
                                    gram_ps[:, :, 0:HALF * F].rearrange("p h (s j) -> p j h s", j=F),
                                    ).then_inc(regrouped, 1)
                dve.wait_ge(regrouped, t + 1)
                nc.vector.tensor_copy(pairs[:, 0:EARLY, :], window(0, EARLY)).then_inc(early_ready, 1)

                dve.wait_ge(paired, t + 1)
                whole = BLOCKS - 1
                nc.vector.tensor_copy(zT[:, 0:whole, bass.ds(t * P, P)],
                                      pair_ps[:, 0:whole * P].rearrange("p (c b) -> p c b", c=whole))
                nc.vector.tensor_copy(zT[0:DENSE_AT, whole, bass.ds(t * P, P)],
                                      pair_ps[0:DENSE_AT, whole * P:BLOCKS * P]).then_inc(z_ready, 1)

                dve.wait_ge(l2_done, t + 1)
                for m in range(M2):
                    last = nc.vector.tensor_scalar(h2T[:, m, :], h2_ps[:, m * P:(m + 1) * P],
                                                   b2_sb[:, m:m + 1], 0.0, ALU.add, ALU.max)
                last.then_inc(h2_ready, 1)

        @block.scalar
        def _(act):
            act.wait_ge(small_in, 16)
            with act.Fori(0, TILES) as t:
                for g in range(NG):
                    if not on_vector(g):
                        act.wait_ge(turned, t * NG + g + 1)
                        dst, src = group_out(g)
                        nc.scalar.copy(dst, src).then_inc(taken_s, 1)

                act.wait_ge(regrouped, t + 1)
                nc.scalar.copy(gram[:, F:F + STEPS, STEPS:F], gram[:, 0:STEPS, STEPS:F]).then_inc(repeated, 1)
                act.wait_ge(repeated, t + 1)
                nc.scalar.copy(pairs[:, EARLY:F, :], window(EARLY, F)).then_inc(late_ready, 1)

                act.wait_ge(l1_done, t + 1)
                for m in range(M1):
                    last = nc.scalar.activation(h1T[:, m, :], h1_ps[:, m * P:(m + 1) * P], ACT.Relu,
                                                bias=b1_sb[:, m:m + 1])
                last.then_inc(h1_ready, 1)

                act.wait_ge(l3_done, t + 1)
                nc.scalar.copy(y_sb[0:1, bass.ds(t * P, P)], y_ps).then_inc(y_ready, 1)


def kernel(**inputs):
    import concourse.bacc as bacc
    import numpy as np
    from concourse.bass_utils import run_bass_kernel_spmd

    order = []
    for a in range(F):
        for k in range(1, STEPS + 1):
            low, high = sorted((a, (a + k) % F))
            order.append(high * (high - 1) // 2 + low)
    order += range(PAIRS, PAIRS + DENSE)

    ids = np.asarray(inputs["ids"])
    w1 = np.asarray(inputs["W_top1"])
    b1, b2, w3 = (np.asarray(inputs[n]) for n in ("b_top1", "b_top2", "W_top3"))
    arrays = {
        "ids": np.ascontiguousarray(ids.reshape(TILES, P, F).transpose(1, 0, 2)).reshape(P, TILES * F),
        **{f"tbl_{f}": np.asarray(inputs[f"tbl_{f}"]) for f in range(F)},
        "w1": np.ascontiguousarray(w1[order]),
        "w2": np.asarray(inputs["W_top2"]),
        "small": np.concatenate([x.reshape(-1, P).T for x in (b1, b2, w3)], axis=1),
        "denseT": np.ascontiguousarray(np.asarray(inputs["dense_ctx"]).T),
    }
    nc = bacc.Bacc("TRN2", target_bir_lowering=False, num_devices=1)
    at = {n: nc.dram_tensor(n, a.shape, mybir.dt.from_np(a.dtype), kind="ExternalInput").ap()
          for n, a in arrays.items()}
    out = nc.dram_tensor("y", (1, B), F32, kind="ExternalOutput").ap()
    build(nc, at["ids"], [at[f"tbl_{f}"] for f in range(F)], at["w1"], at["w2"], at["small"], at["denseT"], out)
    result = run_bass_kernel_spmd(nc, [arrays], core_ids=[0])
    return result.results[0]["y"].reshape(B, 1)
```

```python
from contextlib import ExitStack

import concourse.bass as bass
from concourse import mybir

F32 = mybir.dt.float32
F32R = mybir.dt.float32r
I32 = mybir.dt.int32
ALU = mybir.AluOpType
ACT = mybir.ActivationFunctionType

B, F, D = 512, 27, 128
DENSE, H1, H2 = 16, 512, 256
P = 128
STRIP = 32
BANK = 512
M1, M2 = H1 // P, H2 // P

TILES = [(b, P) for b in range(0, B, P)]

FOUND = [1, 2, 8, 12, 15, 17, 18]
NF = len(FOUND)
ROWS, ROWS_EACH = 1000, 8
TP = ROWS // ROWS_EACH
TP_EVEN = TP // 16 * 16
GATHERED = [f for f in range(F) if f not in FOUND]
PLACES = GATHERED + FOUND
NG = len(GATHERED)
PHASES = [(0, 256), (256, 256)]
HALF = ROWS_EACH // 2
UNITS = [(ph, k, h) for ph in range(len(PHASES)) for k in range(NF) for h in range(2)]
MARK_BUFS, RAW_BUFS, ROW_BUFS = 3, 2, 2

PER_BANK = BANK // P
GROUPS = [list(range(g, min(g + PER_BANK, NG))) for g in range(0, NG, PER_BANK)]
TURN_BANKS = 2

K_STEPS = (F - 1) // 2
PAIRS = F * K_STEPS
BLOCKS = -(-(PAIRS + DENSE) // P)
PAIRS_IN = [min(P, PAIRS - c * P) for c in range(BLOCKS)]
K_IN = [min(P, PAIRS + DENSE - c * P) for c in range(BLOCKS)]
DENSE_AT = PAIRS_IN[-1]
EARLY = P // K_STEPS + 1


def steps():
    turns = [[("turn", i, g) for g in range(len(GROUPS))] for i in range(len(TILES))]

    def find(n):
        more = [("spread", n + 2)] if n + 2 < len(PHASES) * NF else []
        return [("find", n)] + more

    order = [("spread", 0), ("spread", 1)]
    for n in range(NF):
        order += find(n)
        if n % 2 == 1 or n >= NF - 3:
            order += turns[0][:1]
            del turns[0][:1]
    order += turns[0] + [("gram", 0)]
    later = [find(NF + n) for n in range(NF)]
    for i in range(len(TILES)):
        if i:
            order += [("gram", i)]
        f = [sum(later[(3 * i + x) * NF // 6:(3 * i + x + 1) * NF // 6], []) for x in range(3)]
        t = turns[i + 1] if i + 1 < len(TILES) else []
        order += t[:1] + f[0] + [("pairs", i)] + t[1:3] + f[1] + [("l1", i)] + t[3:4] + f[2]
        order += [("l2", i)] + t[4:] + [("l3", i)]
    return order


STEPS = steps()
RING = [s for s in STEPS if s[0] in ("find", "turn")]
TURNS = [s for s in STEPS if s[0] == "turn"]


def marks_order():
    made, used, before = 0, 0, []
    for s in STEPS:
        n = min(len(UNITS), used + MARK_BUFS)
        before.append(UNITS[made:n])
        made = max(made, n)
        used += 2 * (s[0] == "find")
    return before


def build(nc, ids, found_ids, tables, w1, w2, small, denseT, out):
    ctx = ExitStack()
    with ctx:
        def sb(name, shape, dt=F32):
            return ctx.enter_context(nc.sbuf_tensor(name, shape, dt))

        def pb(name, shape):
            return ctx.enter_context(nc.psum_tensor(name, shape, F32))

        def sem(name):
            return ctx.enter_context(nc.semaphore(name))

        ids_sb = sb("ids_sb", [P, len(TILES) * NG], I32)
        rows = sb("rows", [P, ROW_BUFS, NG, D])
        rowsT = sb("rowsT", [P, B * F + STRIP - F])
        rowsT_f = rowsT[:, 0:B * F].rearrange("p (b f) -> p f b", f=F)

        raw = sb("raw", [TP, RAW_BUFS, ROWS_EACH * D])
        high = sb("high", [TP, NF, ROWS_EACH * D], F32R)
        low = sb("low", [TP, NF, ROWS_EACH * D], F32R)
        fids = sb("fids", [NF, B], I32)
        fids_r = sb("fids_r", [NF, B], F32R)
        pick = sb("pick", [NF, NF, P], F32R)
        row_no_i = sb("row_no_i", [P, ROWS_EACH], I32)
        row_no = sb("row_no", [P, ROWS_EACH])
        MARK_N = max(n for _, n in PHASES)
        marks = sb("marks", [TP, MARK_BUFS, HALF, MARK_N], F32R)

        gram = sb("gram", [P, F + K_STEPS, STRIP])
        pairs = sb("pairs", [P, F, K_STEPS])
        pairs_flat = pairs[:, :, :].rearrange("p a k -> p (a k)")
        zT = sb("zT", [P, BLOCKS, B])
        w1_sb = sb("w1_sb", [P, BLOCKS, H1])
        w2_sb = sb("w2_sb", [P, M1, H2])
        small_sb = sb("small_sb", [P, M1 + M2 + M2])
        b1_sb, b2_sb, w3_sb = small_sb[:, 0:M1], small_sb[:, M1:M1 + M2], small_sb[:, M1 + M2:]
        h1T = sb("h1T", [P, M1, P])
        h2T = sb("h2T", [P, M2, P])
        y_sb = sb("y_sb", [1, B])
        ident = sb("ident", [P, P])

        turn_ps = pb("turn_ps", [P, TURN_BANKS, BANK])
        ids_ps = pb("ids_ps", [P, 2, BANK])
        gram_ps = pb("gram_ps", [P, STRIP, STRIP])
        chain_a = pb("chain_a", [P, BANK])
        chain_b = pb("chain_b", [P, BANK])

        ids_in = sem("ids_in")
        fids_in = sem("fids_in")
        raw_in = [sem(f"raw_in{r}") for r in range(RAW_BUFS)]
        w1_in = sem("w1_in")
        w2_in = sem("w2_in")
        small_in = sem("small_in")
        dense_in = sem("dense_in")
        ident_zero = sem("ident_zero")
        ident_ready = sem("ident_ready")
        row_no_made = sem("row_no_made")
        row_no_ready = sem("row_no_ready")
        pad_ready = sem("pad_ready")
        pick_ready = sem("pick_ready")
        fids_ready = sem("fids_ready")
        row_in = [[sem(f"row_in{r}_{s}") for s in range(NG)] for r in range(ROW_BUFS)]
        high_ready = sem("high_ready")
        low_ready = sem("low_ready")
        spread = sem("spread")
        marked = sem("marked")
        marks_used = sem("marks_used")
        turned = sem("turned")
        taken = sem("taken")
        products = sem("products")
        regrouped = sem("regrouped")
        repeated = sem("repeated")
        early_ready = sem("early_ready")
        late_ready = sem("late_ready")
        paired = sem("paired")
        z_ready = sem("z_ready")
        l1_done = sem("l1_done")
        h1_ready = sem("h1_ready")
        l2_done = sem("l2_done")
        h2_ready = sem("h2_ready")
        l3_done = sem("l3_done")
        y_ready = sem("y_ready")
        out_done = sem("out_done")

        def phase_of(n):
            return *PHASES[n // NF], n % NF

        def window(n, a0, a1):
            flat = gram[0:n, :, :].rearrange("p j i -> p (j i)")
            start = flat[:, (a0 + 1) * STRIP + a0:]
            return bass.AP(start.tensor, start.offset,
                           [list(start.ap[0]), [STRIP + 1, a1 - a0], [STRIP, K_STEPS]])

        block = ctx.enter_context(nc.Block())

        @block.sync
        def _(sp):
            sp.dma_start(ids_sb[:, :], ids).then_inc(ids_in, 16)
            sp.dma_start(fids[:, :], found_ids).then_inc(fids_in, 16)
            for k, f in enumerate(FOUND):
                if k >= RAW_BUFS:
                    sp.wait_ge(low_ready, k - RAW_BUFS + 1)
                whole = tables[f].rearrange("(p r) d -> p (r d)", r=ROWS_EACH)
                for p0, p1 in ((0, TP_EVEN), (TP_EVEN, TP)):
                    sp.dma_start(raw[p0:p1, k % RAW_BUFS, :], whole[p0:p1, :]).then_inc(raw_in[k % RAW_BUFS], 16)
                if k == 1:
                    sp.dma_start(small_sb[:, :], small).then_inc(small_in, 16)
            sp.dma_start(zT[DENSE_AT:DENSE_AT + DENSE, BLOCKS - 1, :], denseT).then_inc(dense_in, 16)
            for c in range(BLOCKS):
                sp.dma_start(w1_sb[0:K_IN[c], c, :], w1[c * P:c * P + K_IN[c], :]).then_inc(w1_in, 16)
            sp.dma_start(w2_sb[:, :, :], w2.rearrange("(m p) n -> p m n", p=P)).then_inc(w2_in, 16)
            sp.wait_ge(y_ready, len(TILES))
            sp.dma_start(out, y_sb[:, :]).then_inc(out_done, 16)
            sp.wait_ge(out_done, 16)

        @block.gpsimd
        def _(pool):
            nc.gpsimd.memset(ident[:, :], 0.0).then_inc(ident_zero, 1)
            pool.wait_ge(ident_zero, 1)
            nc.gpsimd.affine_select(out=ident[:, :], in_=ident[:, :], compare_op=ALU.not_equal, fill=1.0,
                                    base=0, pattern=[[-1, P]], channel_multiplier=1).then_inc(ident_ready, 1)
            nc.gpsimd.iota(row_no_i[:, :], pattern=[[1, ROWS_EACH]], base=0,
                           channel_multiplier=ROWS_EACH).then_inc(row_no_made, 1)
            for i, (_, n) in enumerate(TILES):
                if i == 0:
                    pool.wait_ge(ids_in, 16)
                for s, f in enumerate(GATHERED):
                    if i >= ROW_BUFS and s % PER_BANK == 0:
                        pool.wait_ge(turned, TURNS.index(("turn", i - ROW_BUFS, s // PER_BANK)) + 1)
                    nc.gpsimd.indirect_dma_start(
                        out=rows[0:n, i % ROW_BUFS, s, :], out_offset=None, in_=tables[f],
                        in_offset=bass.IndirectOffsetOnAxis(ap=ids_sb[0:n, i * NG + s:i * NG + s + 1], axis=0),
                    ).then_inc(row_in[i % ROW_BUFS][s], 16)

        @block.tensor
        def _(pe):
            def use_ring(step):
                e = RING.index(step)
                if e >= TURN_BANKS:
                    pe.wait_ge(taken, e - TURN_BANKS + 1)
                return turn_ps[:, e % TURN_BANKS, :]

            pe.wait_ge(ident_ready, 1)
            pe.wait_ge(pad_ready, 1)
            in_ring = 0
            for step in STEPS:
                kind, i = step[:2]
                in_ring += kind in ("find", "turn")
                if kind == "spread":
                    b0, n, k = phase_of(i)
                    if i == 0:
                        pe.wait_ge(fids_ready, 1)
                        pe.wait_ge(pick_ready, 1)
                    if i >= 2:
                        pe.wait_ge(marked, 2 * (i - 1))
                    nc.tensor.matmul(ids_ps[:, i % 2, 0:n], pick[:, k, :], fids_r[:, b0:b0 + n],
                                     start=True, stop=True).then_inc(spread, 1)

                elif kind == "find":
                    _, n, k = phase_of(i)
                    bank = use_ring(step)
                    if i < NF:
                        pe.wait_ge(low_ready, k + 1)
                    for h in range(2):
                        u = 2 * i + h
                        pe.wait_ge(marked, u + 1)
                        for c in range(HALF):
                            at = (h * HALF + c) * D
                            for part in (high, low):
                                last = nc.tensor.matmul(
                                    bank[:, 0:n], part[:, k, at:at + D], marks[:, u % MARK_BUFS, c, 0:n],
                                    start=h == 0 and c == 0 and part is high,
                                    stop=h == 1 and c == HALF - 1 and part is low)
                        last.then_inc(marks_used, 1)

                elif kind == "turn":
                    n = TILES[i][1]
                    bank = use_ring(step)
                    for m, s in enumerate(GROUPS[step[2]]):
                        pe.wait_ge(row_in[i % ROW_BUFS][s], 16 * (i // ROW_BUFS + 1))
                        last = nc.tensor.transpose(bank[:, m * n:(m + 1) * n],
                                                   rows[0:n, i % ROW_BUFS, s, :], ident[0:n, 0:n])
                    last.then_inc(turned, 1)

                elif kind == "gram":
                    b0, n = TILES[i]
                    pe.wait_ge(taken, in_ring)
                    if i >= 1:
                        pe.wait_ge(regrouped, i)
                    for g in range(STRIP):
                        for s in range(n // STRIP):
                            at = (b0 + s * STRIP + g) * F
                            strip = rowsT[:, at:at + STRIP]
                            last = nc.tensor.matmul(gram_ps[s * STRIP:(s + 1) * STRIP, g, :], strip, strip,
                                                    start=True, stop=True)
                    last.then_inc(products, 1)

                elif kind == "pairs":
                    n = TILES[i][1]
                    pe.wait_ge(early_ready, i + 1)
                    for c in range(BLOCKS):
                        if c == 1:
                            pe.wait_ge(late_ready, i + 1)
                        last = nc.tensor.transpose(chain_a[0:PAIRS_IN[c], c * P:c * P + n],
                                                   pairs_flat[0:n, c * P:c * P + PAIRS_IN[c]],
                                                   ident[0:n, 0:n])
                    last.then_inc(paired, 1)

                elif kind == "l1":
                    b0, n = TILES[i]
                    pe.wait_ge(z_ready, i + 1)
                    if i == 0:
                        pe.wait_ge(w1_in, 16 * BLOCKS)
                        pe.wait_ge(dense_in, 16)
                    else:
                        pe.wait_ge(y_ready, i)
                    for m in range(M1):
                        for c in range(BLOCKS):
                            last = nc.tensor.matmul(chain_b[:, m * P:m * P + n],
                                                    w1_sb[0:K_IN[c], c, m * P:(m + 1) * P],
                                                    zT[0:K_IN[c], c, b0:b0 + n],
                                                    start=c == 0, stop=c == BLOCKS - 1)
                    last.then_inc(l1_done, 1)

                elif kind == "l2":
                    n = TILES[i][1]
                    if i == 0:
                        pe.wait_ge(w2_in, 16)
                    for m in range(M2):
                        for c in range(M1):
                            if m == 0:
                                pe.wait_ge(h1_ready, M1 * i + c + 1)
                            last = nc.tensor.matmul(chain_a[:, m * P:m * P + n],
                                                    w2_sb[:, c, m * P:(m + 1) * P], h1T[:, c, 0:n],
                                                    start=c == 0, stop=c == M1 - 1)
                    last.then_inc(l2_done, 1)

                elif kind == "l3":
                    n = TILES[i][1]
                    pe.wait_ge(h2_ready, i + 1)
                    for c in range(M2):
                        last = nc.tensor.matmul(chain_b[0:1, 0:n], w3_sb[:, c:c + 1], h2T[:, c, 0:n],
                                                start=c == 0, stop=c == M2 - 1)
                    last.then_inc(l3_done, 1)

        @block.vector
        def _(dve):
            for b0, n in TILES:
                last = nc.vector.memset(rowsT[:, (b0 + n) * F:(b0 + n) * F + STRIP - F], 0.0)
            last.then_inc(pad_ready, 1)
            dve.wait_ge(ident_ready, 1)
            nc.vector.tensor_copy(pick[:, :, :], ident[0:NF, 0:NF].rearrange("p (k o) -> p k o", o=1)
                                  .to_broadcast([NF, NF, P])).then_inc(pick_ready, 1)
            dve.wait_ge(row_no_made, 1)
            nc.vector.tensor_copy(row_no[:, :], row_no_i[:, :]).then_inc(row_no_ready, 1)
            dve.wait_ge(fids_in, 16)
            nc.vector.tensor_copy(fids_r[:, :], fids[:, :]).then_inc(fids_ready, 1)
            dve.wait_ge(row_no_ready, 1)

            def mark(ph, k, h):
                n = PHASES[ph][1]
                t = ph * NF + k
                u = 2 * t + h
                if ph == 0 and h == 0:
                    dve.wait_ge(high_ready, k + 1)
                    nc.vector.tensor_tensor(low[:, k, :], raw[:, k % RAW_BUFS, :], high[:, k, :].bitcast(F32),
                                            ALU.subtract).then_inc(low_ready, 1)
                if h == 0:
                    dve.wait_ge(spread, t + 1)
                if u >= MARK_BUFS:
                    dve.wait_ge(marks_used, u - MARK_BUFS + 1)
                which = row_no[0:TP, h * HALF:(h + 1) * HALF].rearrange("p (c o) -> p c o", o=1)
                index = ids_ps[0:TP, t % 2, 0:n].rearrange("p (o b) -> p o b", o=1)
                nc.vector.tensor_tensor(marks[:, u % MARK_BUFS, :, 0:n],
                                        index.to_broadcast([TP, HALF, n]), which.to_broadcast([TP, HALF, n]),
                                        ALU.is_equal).then_inc(marked, 1)

            for (kind, i, *_), units in zip(STEPS, marks_order()):
                for unit in units:
                    mark(*unit)
                if kind == "gram":
                    n = TILES[i][1]
                    dve.wait_ge(products, i + 1)
                    if i >= 1:
                        dve.wait_ge(late_ready, i)
                    nc.vector.transpose(gram[0:n, 0:F, :], gram_ps[0:n, :, 0:F].rearrange("p s j -> p j s"),
                                        ).then_inc(regrouped, 1)
                    dve.wait_ge(regrouped, i + 1)
                    if i >= 1:
                        dve.wait_ge(paired, i)
                    nc.vector.tensor_copy(pairs[0:n, 0:EARLY, :], window(n, 0, EARLY)).then_inc(early_ready, 1)
                elif kind == "pairs":
                    b0, n = TILES[i]
                    dve.wait_ge(paired, i + 1)
                    full = BLOCKS - 1
                    nc.vector.tensor_copy(zT[:, 0:full, b0:b0 + n],
                                          chain_a[:, 0:full * P].rearrange("p (c b) -> p c b", c=full)[:, :, 0:n])
                    nc.vector.tensor_copy(zT[0:DENSE_AT, full, b0:b0 + n],
                                          chain_a[0:DENSE_AT, full * P:full * P + n]).then_inc(z_ready, 1)

        @block.scalar
        def _(act):
            def split(k):
                act.wait_ge(raw_in[k % RAW_BUFS], 32 * (k // RAW_BUFS + 1))
                nc.scalar.copy(high[:, k, :], raw[:, k % RAW_BUFS, :]).then_inc(high_ready, 1)

            split(0)
            finds = turns = 0
            for step in STEPS:
                kind, i = step[:2]
                if kind == "find":
                    b0, n, k = phase_of(i)
                    if i + 1 < NF:
                        split(i + 1)
                    finds += 1
                    act.wait_ge(marks_used, 2 * finds)
                    nc.scalar.copy(rowsT_f[:, NG + k, b0:b0 + n],
                                   turn_ps[:, RING.index(step) % TURN_BANKS, 0:n]).then_inc(taken, 1)
                elif kind == "turn":
                    b0, n = TILES[i]
                    group = GROUPS[step[2]]
                    turns += 1
                    act.wait_ge(turned, turns)
                    src = turn_ps[:, RING.index(step) % TURN_BANKS, 0:len(group) * n]
                    nc.scalar.copy(rowsT_f[:, group[0]:group[-1] + 1, b0:b0 + n],
                                   src.rearrange("p (f b) -> p f b", b=n)).then_inc(taken, 1)
                elif kind == "pairs":
                    n = TILES[i][1]
                    act.wait_ge(regrouped, i + 1)
                    nc.scalar.copy(gram[0:n, F:F + K_STEPS, K_STEPS:F],
                                   gram[0:n, 0:K_STEPS, K_STEPS:F]).then_inc(repeated, 1)
                    act.wait_ge(repeated, i + 1)
                    nc.scalar.copy(pairs[0:n, EARLY:F, :], window(n, EARLY, F)).then_inc(late_ready, 1)
                elif kind == "l1":
                    n = TILES[i][1]
                    if i == 0:
                        act.wait_ge(small_in, 16)
                    act.wait_ge(l1_done, i + 1)
                    for m in range(M1):
                        nc.scalar.activation(h1T[:, m, 0:n], chain_b[:, m * P:m * P + n], ACT.Relu,
                                             bias=b1_sb[:, m:m + 1]).then_inc(h1_ready, 1)
                elif kind == "l2":
                    n = TILES[i][1]
                    act.wait_ge(l2_done, i + 1)
                    for m in range(M2):
                        last = nc.scalar.activation(h2T[:, m, 0:n], chain_a[:, m * P:m * P + n], ACT.Relu,
                                                    bias=b2_sb[:, m:m + 1])
                    last.then_inc(h2_ready, 1)
                elif kind == "l3":
                    b0, n = TILES[i]
                    act.wait_ge(l3_done, i + 1)
                    nc.scalar.copy(y_sb[0:1, b0:b0 + n], chain_b[0:1, 0:n]).then_inc(y_ready, 1)


def kernel(**inputs):
    import concourse.bacc as bacc
    import numpy as np
    from concourse.bass_utils import run_bass_kernel_spmd

    order = []
    for a in range(F):
        for k in range(1, K_STEPS + 1):
            low, high = sorted((PLACES[a], PLACES[(a + k) % F]))
            order.append(high * (high - 1) // 2 + low)
    order += range(PAIRS, PAIRS + DENSE)

    ids = np.asarray(inputs["ids"])
    w1 = np.asarray(inputs["W_top1"])
    b1, b2, w3 = (np.asarray(inputs[n]) for n in ("b_top1", "b_top2", "W_top3"))

    arrays = {
        "ids": np.concatenate([ids[b0:b0 + n, GATHERED] for b0, n in TILES], axis=1),
        "found_ids": np.ascontiguousarray(ids[:, FOUND].T),
        **{f"tbl_{f}": np.asarray(inputs[f"tbl_{f}"]) for f in range(F)},
        "w1": np.ascontiguousarray(w1[order]),
        "w2": np.asarray(inputs["W_top2"]),
        "small": np.concatenate([x.reshape(-1, P).T for x in (b1, b2, w3)], axis=1),
        "denseT": np.ascontiguousarray(np.asarray(inputs["dense_ctx"]).T),
    }
    nc = bacc.Bacc("TRN2", target_bir_lowering=False, num_devices=1)
    at = {n: nc.dram_tensor(n, a.shape, mybir.dt.from_np(a.dtype), kind="ExternalInput").ap()
          for n, a in arrays.items()}
    out = nc.dram_tensor("y", (1, B), F32, kind="ExternalOutput").ap()
    build(nc, at["ids"], at["found_ids"], [at[f"tbl_{f}"] for f in range(F)],
          at["w1"], at["w2"], at["small"], at["denseT"], out)
    result = run_bass_kernel_spmd(nc, [arrays], core_ids=[0])
    return result.results[0]["y"].reshape(B, 1)
```

```python
from contextlib import ExitStack

import concourse.bass as bass
from concourse import mybir

F32 = mybir.dt.float32
F32R = mybir.dt.float32r
I32 = mybir.dt.int32
ALU = mybir.AluOpType
ACT = mybir.ActivationFunctionType

B, F, D = 512, 27, 128
DENSE, H1, H2 = 16, 512, 256
P = 128
STRIP = 32
BANK = 512
M1, M2 = H1 // P, H2 // P

TILES = [(b, P) for b in range(0, B, P)]

ROWS, ROWS_EACH = 1000, 8
TP = ROWS // ROWS_EACH
TP_EVEN = TP // 16 * 16
FOUND = [(1, 0), (2, 0), (8, 0), (12, 0), (15, 0), (17, 128), (18, 128), (22, 128), (23, 128), (25, 256)]
JOBS = [(s0, B - s0) for _, s0 in FOUND]
NEEDED = [len([1 for s0, _ in JOBS if s0 <= b0]) for b0, _ in TILES]
MARK_SIZE = 1024


def rows_in_unit(n):
    return 1 << (MARK_SIZE // n).bit_length() - 1


UNITS = [(j, c, c + rows_in_unit(n)) for j, (_, n) in enumerate(JOBS)
         for c in range(0, ROWS_EACH, rows_in_unit(n))]
HELPED = 4
BY_ACT = [u for u in UNITS if u[0] < HELPED and u[2] == ROWS_EACH]
BY_DVE = [u for u in UNITS if u not in BY_ACT]
MARK_BUFS, RAW_BUFS, SPLIT_BUFS, ROW_BUFS = 8, 3, 3, 2


def units_of(j):
    return [u for u in UNITS if u[0] == j]


def through(units, j):
    return len([u for u in units if u[0] <= j])


PLACES = [f for f in range(F) if f not in [x for x, _ in FOUND]] + [f for f, _ in FOUND[::-1]]


def place_of(j):
    return F - 1 - j


N_GATHERED = [F - n for n in NEEDED]
SLOTS = max(N_GATHERED)
AT_ID = [sum(N_GATHERED[:i]) for i in range(len(TILES))]

PER_BANK = BANK // P
GROUPS = [[range(g, min(g + PER_BANK, ng)) for g in range(0, ng, PER_BANK)] for ng in N_GATHERED]
TURN_BANKS = 2
GRAM_BANKS = 2

K_STEPS = (F - 1) // 2
PAIRS = F * K_STEPS
BLOCKS = -(-(PAIRS + DENSE) // P)
PAIRS_IN = [min(P, PAIRS - c * P) for c in range(BLOCKS)]
K_IN = [min(P, PAIRS + DENSE - c * P) for c in range(BLOCKS)]
DENSE_AT = PAIRS_IN[-1]
PART_BLOCKS = [[0], list(range(1, BLOCKS))]
EARLY = P // K_STEPS + 1


WARM_START, WARM_ROWS, WARM_LAST = (4, 5), 6, 5


def steps():
    turns = [[("turn", i, g) for g in range(len(GROUPS[i]))] for i in range(len(TILES))]

    order = []
    for j in range(NEEDED[0]):
        order += [("find", j), turns[0].pop(0)]
    order += turns[0]
    for i in range(len(TILES)):
        t = turns[i + 1] if i + 1 < len(TILES) else []
        lo, hi = NEEDED[i], NEEDED[min(i + 1, len(TILES) - 1)]
        cut = [lo + (hi - lo) * x // 3 for x in range(4)]
        f = [[("find", j) for j in range(cut[x], cut[x + 1])] for x in range(3)]
        l2 = [("l2", i - 1)] if 0 < i < len(TILES) - 1 else []
        l3 = [("l3", i - 1)] if i else []
        if i + 1 < len(TILES):
            order += [("gram", i, 0)] + t[:1] + [("gram", i, 1)] + l2 + f[0] + t[1:2] + l3
        else:
            order += [("gram", i, 0)] + l3 + [("gram", i, 1), ("warm", WARM_LAST)]
        order += [("pairs", i, 0)] + t[2:3] + [("pairs", i, 1)] + f[1]
        if i + 2 < len(TILES):
            order += t[3:4] + f[2] + t[4:] + [("l1", i)]
        else:
            order += [("l1", i)] + t[3:4] + [("l2", i)] + t[4:]
    order += [("l3", i)]
    return order


STEPS = steps()
RING = [s for s in STEPS if s[0] in ("find", "turn")]
FIRST_RING = len([s for s in STEPS[:STEPS.index(("gram", 0, 0))] if s in RING])
TURNS = [s for s in STEPS if s[0] == "turn"]


def marks_order():
    made, used, before = 0, 0, []
    for s in STEPS:
        n = min(len(UNITS), used + MARK_BUFS)
        before.append(UNITS[made:n])
        made = max(made, n)
        if s[0] == "find":
            used += len(units_of(s[1]))
    return before


def build(nc, ids, found_ids, tables, w1, w2, small, denseT, out):
    ctx = ExitStack()
    with ctx:
        def sb(name, shape, dt=F32):
            return ctx.enter_context(nc.sbuf_tensor(name, shape, dt))

        def pb(name, shape):
            return ctx.enter_context(nc.psum_tensor(name, shape, F32))

        def sem(name):
            return ctx.enter_context(nc.semaphore(name))

        ids_sb = sb("ids_sb", [P, sum(N_GATHERED)], I32)
        rows = sb("rows", [P, ROW_BUFS, SLOTS, D])
        rowsT = sb("rowsT", [P, B * F])
        rowsT_f = rowsT[:, :].rearrange("p (b f) -> p f b", f=F)

        raw = sb("raw", [TP, RAW_BUFS, ROWS_EACH * D])
        high = sb("high", [TP, SPLIT_BUFS, ROWS_EACH * D], F32R)
        low = sb("low", [TP, SPLIT_BUFS, ROWS_EACH * D], F32R)
        fids = sb("fids", [len(FOUND), B], I32)
        fids_r = sb("fids_r", [len(FOUND), B], F32R)
        pick = sb("pick", [len(FOUND), len(FOUND), P], F32R)
        row_no_i = sb("row_no_i", [P, ROWS_EACH], I32)
        row_no = sb("row_no", [P, ROWS_EACH])
        away = sb("away", [TP, MARK_SIZE])
        marks = sb("marks", [TP, MARK_BUFS, MARK_SIZE], F32R)

        gram = sb("gram", [P, F + K_STEPS, STRIP])
        pairs = sb("pairs", [P, F, K_STEPS])
        pairs_flat = pairs[:, :, :].rearrange("p a k -> p (a k)")
        zT = sb("zT", [P, BLOCKS, B])
        w1_sb = sb("w1_sb", [P, BLOCKS, H1])
        w2_sb = sb("w2_sb", [P, M1, H2])
        small_sb = sb("small_sb", [P, M1 + M2 + M2])
        b1_sb, b2_sb, w3_sb = small_sb[:, 0:M1], small_sb[:, M1:M1 + M2], small_sb[:, M1 + M2:]
        h1T = sb("h1T", [P, M1, P])
        h2T = sb("h2T", [P, M2, P])
        y_sb = sb("y_sb", [1, B])
        ident = sb("ident", [P, P])

        turn_ps = pb("turn_ps", [P, TURN_BANKS, BANK])
        ids_ps = pb("ids_ps", [P, 2, BANK])
        gram_ps = pb("gram_ps", [P, STRIP, STRIP])
        chain = pb("chain", [P, 2, BANK])

        ids_in = sem("ids_in")
        fids_in = sem("fids_in")
        raw_in = [sem(f"raw_in{r}") for r in range(RAW_BUFS)]
        w1_in = sem("w1_in")
        w2_in = sem("w2_in")
        small_in = sem("small_in")
        dense_in = sem("dense_in")
        ident_zero = sem("ident_zero")
        ident_ready = sem("ident_ready")
        row_no_made = sem("row_no_made")
        row_no_ready = sem("row_no_ready")
        gram_cleared = sem("gram_cleared")
        pick_ready = sem("pick_ready")
        fids_ready = sem("fids_ready")
        row_in = [[sem(f"row_in{r}_{s}") for s in range(SLOTS)] for r in range(ROW_BUFS)]
        high_ready = sem("high_ready")
        low_ready = sem("low_ready")
        spread = sem("spread")
        marked = sem("marked")
        marked_too = sem("marked_too")
        away_ready = sem("away_ready")
        marks_used = sem("marks_used")
        turned = sem("turned")
        taken = sem("taken")
        products = sem("products")
        regrouped = sem("regrouped")
        repeated = sem("repeated")
        early_ready = sem("early_ready")
        late_ready = sem("late_ready")
        paired = sem("paired")
        z_ready = sem("z_ready")
        l1_done = sem("l1_done")
        h1_ready = sem("h1_ready")
        l2_done = sem("l2_done")
        h2_ready = sem("h2_ready")
        l3_done = sem("l3_done")
        y_ready = sem("y_ready")
        out_done = sem("out_done")

        def ring_bank(step):
            e = RING.index(step)
            if e < FIRST_RING and e % (TURN_BANKS + GRAM_BANKS) >= TURN_BANKS:
                at = (e % (TURN_BANKS + GRAM_BANKS) - TURN_BANKS) * STRIP // GRAM_BANKS
                return gram_ps[:, at:at + STRIP // GRAM_BANKS, :].rearrange("p g j -> p (g j)")
            return turn_ps[:, e % (TURN_BANKS + GRAM_BANKS if e < FIRST_RING else TURN_BANKS), :]

        def mark_of(unit, c):
            n = JOBS[unit[0]][1]
            return marks[:, UNITS.index(unit) % MARK_BUFS, (c - unit[1]) * n:(c - unit[1] + 1) * n]

        def marks_of(unit):
            j, c0, c1 = unit
            return marks[:, UNITS.index(unit) % MARK_BUFS, 0:(c1 - c0) * JOBS[j][1]].rearrange(
                "p (c b) -> p c b", c=c1 - c0)

        def window(n, a0, a1):
            flat = gram[0:n, :, :].rearrange("p j i -> p (j i)")
            start = flat[:, (a0 + 1) * STRIP + a0:]
            return bass.AP(start.tensor, start.offset,
                           [list(start.ap[0]), [STRIP + 1, a1 - a0], [STRIP, K_STEPS]])

        block = ctx.enter_context(nc.Block())

        @block.sync
        def _(sp):
            sp.dma_start(ids_sb[:, :], ids).then_inc(ids_in, 16)
            sp.dma_start(fids[:, :], found_ids).then_inc(fids_in, 16)
            for k, (f, _) in enumerate(FOUND):
                if k >= RAW_BUFS:
                    sp.wait_ge(low_ready, k - RAW_BUFS + 1)
                whole = tables[f].rearrange("(p r) d -> p (r d)", r=ROWS_EACH)
                for p0, p1 in ((0, TP_EVEN), (TP_EVEN, TP)):
                    sp.dma_start(raw[p0:p1, k % RAW_BUFS, :],
                                 whole[p0:p1, :]).then_inc(raw_in[k % RAW_BUFS], 16)
                if k == 1:
                    sp.dma_start(small_sb[:, :], small).then_inc(small_in, 16)
            sp.dma_start(zT[DENSE_AT:DENSE_AT + DENSE, BLOCKS - 1, :], denseT).then_inc(dense_in, 16)
            for c in range(BLOCKS):
                sp.dma_start(w1_sb[0:K_IN[c], c, :], w1[c * P:c * P + K_IN[c], :]).then_inc(w1_in, 16)
            sp.dma_start(w2_sb[:, :, :], w2.rearrange("(m p) n -> p m n", p=P)).then_inc(w2_in, 16)
            sp.wait_ge(y_ready, len(TILES))
            sp.dma_start(out, y_sb[:, :]).then_inc(out_done, 16)
            sp.wait_ge(out_done, 16)

        @block.gpsimd
        def _(pool):
            nc.gpsimd.memset(ident[:, :], 0.0).then_inc(ident_zero, 1)
            pool.wait_ge(ident_zero, 1)
            nc.gpsimd.affine_select(out=ident[:, :], in_=ident[:, :], compare_op=ALU.not_equal, fill=1.0,
                                    base=0, pattern=[[-1, P]], channel_multiplier=1).then_inc(ident_ready, 1)
            nc.gpsimd.iota(row_no_i[:, :], pattern=[[1, ROWS_EACH]], base=0,
                           channel_multiplier=ROWS_EACH).then_inc(row_no_made, 1)
            for i, (_, n) in enumerate(TILES):
                if i == 0:
                    pool.wait_ge(ids_in, 16)
                for s in range(N_GATHERED[i]):
                    if i >= ROW_BUFS and s % PER_BANK == 0:
                        pool.wait_ge(turned, TURNS.index(("turn", i - ROW_BUFS, s // PER_BANK)) + 1)
                    nc.gpsimd.indirect_dma_start(
                        out=rows[0:n, i % ROW_BUFS, s, :], out_offset=None, in_=tables[PLACES[s]],
                        in_offset=bass.IndirectOffsetOnAxis(
                            ap=ids_sb[0:n, AT_ID[i] + s:AT_ID[i] + s + 1], axis=0),
                    ).then_inc(row_in[i % ROW_BUFS][s], 16)

        @block.tensor
        def _(pe):
            def use_ring(step):
                e = RING.index(step)
                banks = TURN_BANKS + GRAM_BANKS if e < FIRST_RING else TURN_BANKS
                if e >= banks:
                    pe.wait_ge(taken, e - banks + 1)
                return ring_bank(step)

            def spread_ids(j):
                b0, n = JOBS[j]
                if j < HELPED:
                    if j >= 2:
                        pe.wait_ge(away_ready, j - 1)
                    nc.tensor.matmul(chain[:, j % 2, 0:n], pick[:, j, :], fids_r[:, b0:b0 + n],
                                     start=True, stop=True)
                if j >= 2:
                    pe.wait_ge(marked, through(BY_DVE, j - 2))
                nc.tensor.matmul(ids_ps[:, j % 2, 0:n], pick[:, j, :], fids_r[:, b0:b0 + n],
                                 start=True, stop=True).then_inc(spread, 1)

            def warm(times, bank):
                for _ in range(times):
                    nc.tensor.matmul(bank[:, 0:P], ident[:, :], ident[:, :], start=True, stop=True)

            pe.wait_ge(ident_ready, 1)
            warm(WARM_START[0], turn_ps[:, 0, :])
            pe.wait_ge(fids_ready, 1)
            pe.wait_ge(pick_ready, 1)
            spread_ids(0)
            spread_ids(1)
            warm(WARM_START[1], turn_ps[:, 0, :])
            pe.wait_ge(gram_cleared, 1)
            in_ring = 0
            for step in STEPS:
                kind, i = step[:2]
                in_ring += kind in ("find", "turn")
                if kind == "find":
                    _, n = JOBS[i]
                    bank = use_ring(step)
                    pe.wait_ge(low_ready, i + 1)
                    for unit in units_of(i):
                        _, c0, c1 = unit
                        if c1 == ROWS_EACH and i + 2 < len(JOBS):
                            spread_ids(i + 2)
                        if unit in BY_ACT:
                            pe.wait_ge(marked_too, BY_ACT.index(unit) + 1)
                        else:
                            pe.wait_ge(marked, BY_DVE.index(unit) + 1)
                        for c in range(c0, c1):
                            for part in (high, low):
                                last = nc.tensor.matmul(
                                    bank[:, 0:n], part[:, i % SPLIT_BUFS, c * D:(c + 1) * D], mark_of(unit, c),
                                    start=c == 0 and part is high, stop=c == ROWS_EACH - 1 and part is low)
                        last.then_inc(marks_used, 1)

                elif kind == "turn":
                    n = TILES[i][1]
                    bank = use_ring(step)
                    if step == ("turn", 0, len(GROUPS[0]) - 1):
                        warm(WARM_ROWS, bank)
                    for m, s in enumerate(GROUPS[i][step[2]]):
                        pe.wait_ge(row_in[i % ROW_BUFS][s], 16 * (i // ROW_BUFS + 1))
                        last = nc.tensor.transpose(bank[:, m * n:(m + 1) * n],
                                                   rows[0:n, i % ROW_BUFS, s, :], ident[0:n, 0:n])
                    last.then_inc(turned, 1)

                elif kind == "gram":
                    b0, n = TILES[i]
                    half = step[2]
                    if half == 0:
                        pe.wait_ge(taken, in_ring)
                        if i >= 1:
                            pe.wait_ge(regrouped, i)
                    for g in range(half * STRIP // 2, (half + 1) * STRIP // 2):
                        for s in range(n // STRIP):
                            at = (b0 + s * STRIP + g) * F
                            places = rowsT[:, at:at + F]
                            last = nc.tensor.matmul(gram_ps[s * STRIP:s * STRIP + F, g, 0:F], places, places,
                                                    start=True, stop=True)
                    if half == 1:
                        last.then_inc(products, 1)

                elif kind == "pairs":
                    n = TILES[i][1]
                    if step[2] == 0:
                        pe.wait_ge(early_ready, i + 1)
                        if i >= 1:
                            pe.wait_ge(y_ready, i)
                    else:
                        pe.wait_ge(late_ready, i + 1)
                    for c in PART_BLOCKS[step[2]]:
                        last = nc.tensor.transpose(chain[0:PAIRS_IN[c], step[2], c * P:c * P + n],
                                                   pairs_flat[0:n, c * P:c * P + PAIRS_IN[c]],
                                                   ident[0:n, 0:n])
                    last.then_inc(paired, 1)

                elif kind == "l1":
                    b0, n = TILES[i]
                    if i == 0:
                        pe.wait_ge(w1_in, 16 * BLOCKS)
                        pe.wait_ge(dense_in, 16)
                    for m in range(M1):
                        if m >= 2:
                            pe.wait_ge(h1_ready, M1 * i + m - 1)
                        for c in range(BLOCKS):
                            if m == 0 and c < 2:
                                pe.wait_ge(z_ready, 2 * i + c + 1)
                            last = nc.tensor.matmul(chain[:, m % 2, m * P:m * P + n],
                                                    w1_sb[0:K_IN[c], c, m * P:(m + 1) * P],
                                                    zT[0:K_IN[c], c, b0:b0 + n],
                                                    start=c == 0, stop=c == BLOCKS - 1)
                        last.then_inc(l1_done, 1)

                elif kind == "l2":
                    n = TILES[i][1]
                    if i == 0:
                        pe.wait_ge(w2_in, 16)
                    pe.wait_ge(h1_ready, M1 * i + M1 - 1)
                    for m in range(M2):
                        for c in range(M1):
                            if m == 0 and c == M1 - 1:
                                pe.wait_ge(h1_ready, M1 * i + M1)
                            last = nc.tensor.matmul(chain[:, m % 2, m * P:m * P + n],
                                                    w2_sb[:, c, m * P:(m + 1) * P], h1T[:, c, 0:n],
                                                    start=c == 0, stop=c == M1 - 1)
                        last.then_inc(l2_done, 1)

                elif kind == "warm":
                    warm(i, turn_ps[:, 0, :])

                elif kind == "l3":
                    n = TILES[i][1]
                    for c in range(M2):
                        pe.wait_ge(h2_ready, M2 * i + c + 1)
                        last = nc.tensor.matmul(chain[0:1, 0, 0:n], w3_sb[:, c:c + 1], h2T[:, c, 0:n],
                                                start=c == 0, stop=c == M2 - 1)
                    last.then_inc(l3_done, 1)

        @block.vector
        def _(dve):
            nc.vector.memset(gram_ps[:, :, :], 0.0).then_inc(gram_cleared, 1)
            dve.wait_ge(ident_ready, 1)
            unit_vectors = ident[0:len(FOUND), 0:len(FOUND)].rearrange("p (k o) -> p k o", o=1)
            nc.vector.tensor_copy(pick[:, :, :], unit_vectors.to_broadcast([len(FOUND), len(FOUND), P])
                                  ).then_inc(pick_ready, 1)
            dve.wait_ge(row_no_made, 1)
            nc.vector.tensor_copy(row_no[:, :], row_no_i[:, :]).then_inc(row_no_ready, 1)
            dve.wait_ge(fids_in, 16)
            nc.vector.tensor_copy(fids_r[:, :], fids[:, :]).then_inc(fids_ready, 1)
            dve.wait_ge(row_no_ready, 1)

            def mark(unit):
                j, c0, c1 = unit
                n = JOBS[j][1]
                u = UNITS.index(unit)
                if c0 == 0:
                    dve.wait_ge(spread, j + 1)
                if u >= MARK_BUFS:
                    dve.wait_ge(marks_used, u - MARK_BUFS + 1)
                which = row_no[0:TP, c0:c1].rearrange("p (c o) -> p c o", o=1)
                index = ids_ps[0:TP, j % 2, 0:n].rearrange("p (o b) -> p o b", o=1)
                nc.vector.tensor_tensor(marks_of(unit), index.to_broadcast([TP, c1 - c0, n]),
                                        which.to_broadcast([TP, c1 - c0, n]), ALU.is_equal).then_inc(marked, 1)
                if c0 == 0:
                    dve.wait_ge(high_ready, j + 1)
                    nc.vector.tensor_tensor(low[:, j % SPLIT_BUFS, :], raw[:, j % RAW_BUFS, :],
                                            high[:, j % SPLIT_BUFS, :].bitcast(F32),
                                            ALU.subtract).then_inc(low_ready, 1)

            for (kind, i, *more), units in zip(STEPS, marks_order()):
                for unit in units:
                    if unit in BY_DVE:
                        mark(unit)
                if kind == "gram" and more[0] == 1:
                    n = TILES[i][1]
                    dve.wait_ge(products, i + 1)
                    if i >= 1:
                        dve.wait_ge(late_ready, i)
                    nc.vector.transpose(gram[0:n, 0:F, :], gram_ps[0:n, :, 0:F].rearrange("p s j -> p j s"),
                                        ).then_inc(regrouped, 1)
                    dve.wait_ge(regrouped, i + 1)
                    if i >= 1:
                        dve.wait_ge(paired, 2 * i)
                    nc.vector.tensor_copy(pairs[0:n, 0:EARLY, :], window(n, 0, EARLY)).then_inc(early_ready, 1)
                elif kind == "pairs":
                    b0, n = TILES[i]
                    dve.wait_ge(paired, 2 * i + more[0] + 1)
                    for c in PART_BLOCKS[more[0]]:
                        last = nc.vector.tensor_copy(zT[0:PAIRS_IN[c], c, b0:b0 + n],
                                                     chain[0:PAIRS_IN[c], more[0], c * P:c * P + n])
                    last.then_inc(z_ready, 1)

        @block.scalar
        def _(act):
            def split(k):
                act.wait_ge(raw_in[k % RAW_BUFS], 32 * (k // RAW_BUFS + 1))
                if k >= SPLIT_BUFS:
                    act.wait_ge(marks_used, through(UNITS, k - SPLIT_BUFS))
                nc.scalar.copy(high[:, k % SPLIT_BUFS, :], raw[:, k % RAW_BUFS, :]).then_inc(high_ready, 1)

            def mark(unit):
                j, c0, c1 = unit
                n = JOBS[j][1]
                u = UNITS.index(unit)
                if j == 0:
                    act.wait_ge(row_no_ready, 1)
                act.wait_ge(spread, j + 1)
                if j >= 1:
                    act.wait_ge(marked_too, j)
                for c in range(c0, c1):
                    last = nc.scalar.activation(away[:, (c - c0) * n:(c - c0 + 1) * n], chain[0:TP, j % 2, 0:n],
                                                ACT.Abs, bias=row_no[0:TP, c:c + 1], scale=-1.0)
                last.then_inc(away_ready, 1)
                act.wait_ge(away_ready, j + 1)
                if u >= MARK_BUFS:
                    act.wait_ge(marks_used, u - MARK_BUFS + 1)
                nc.scalar.activation(marks[:, u % MARK_BUFS, 0:(c1 - c0) * n], away[:, 0:(c1 - c0) * n],
                                     ACT.Relu, bias=1.0, scale=-1.0).then_inc(marked_too, 1)

            split(0)
            turns = 0
            for step, units in zip(STEPS, marks_order()):
                kind, i = step[:2]
                for unit in units:
                    if unit[1] == 0 and unit[0] + 1 < len(JOBS):
                        split(unit[0] + 1)
                    if unit in BY_ACT:
                        mark(unit)
                if kind == "find":
                    b0, n = JOBS[i]
                    act.wait_ge(marks_used, through(UNITS, i))
                    nc.scalar.copy(rowsT_f[:, place_of(i), b0:b0 + n],
                                   ring_bank(step)[:, 0:n]).then_inc(taken, 1)
                elif kind == "turn":
                    b0, n = TILES[i]
                    group = GROUPS[i][step[2]]
                    turns += 1
                    act.wait_ge(turned, turns)
                    src = ring_bank(step)[:, 0:len(group) * n]
                    nc.scalar.copy(rowsT_f[:, group[0]:group[-1] + 1, b0:b0 + n],
                                   src.rearrange("p (f b) -> p f b", b=n)).then_inc(taken, 1)
                elif kind == "gram" and step[2] == 1:
                    n = TILES[i][1]
                    act.wait_ge(regrouped, i + 1)
                    nc.scalar.copy(gram[0:n, F:F + K_STEPS, K_STEPS:F],
                                   gram[0:n, 0:K_STEPS, K_STEPS:F]).then_inc(repeated, 1)
                    act.wait_ge(repeated, i + 1)
                    nc.scalar.copy(pairs[0:n, EARLY:F, :], window(n, EARLY, F)).then_inc(late_ready, 1)
                elif kind == "l1":
                    n = TILES[i][1]
                    if i == 0:
                        act.wait_ge(small_in, 16)
                    for m in range(M1):
                        act.wait_ge(l1_done, M1 * i + m + 1)
                        nc.scalar.activation(h1T[:, m, 0:n], chain[:, m % 2, m * P:m * P + n], ACT.Relu,
                                             bias=b1_sb[:, m:m + 1]).then_inc(h1_ready, 1)
                elif kind == "l2":
                    n = TILES[i][1]
                    for m in range(M2):
                        act.wait_ge(l2_done, M2 * i + m + 1)
                        nc.scalar.activation(h2T[:, m, 0:n], chain[:, m % 2, m * P:m * P + n], ACT.Relu,
                                             bias=b2_sb[:, m:m + 1]).then_inc(h2_ready, 1)
                elif kind == "l3":
                    b0, n = TILES[i]
                    act.wait_ge(l3_done, i + 1)
                    nc.scalar.copy(y_sb[0:1, b0:b0 + n], chain[0:1, 0, 0:n]).then_inc(y_ready, 1)


def kernel(**inputs):
    import concourse.bacc as bacc
    import numpy as np
    from concourse.bass_utils import run_bass_kernel_spmd

    order = []
    for a in range(F):
        for k in range(1, K_STEPS + 1):
            low, high = sorted((PLACES[a], PLACES[(a + k) % F]))
            order.append(high * (high - 1) // 2 + low)
    order += range(PAIRS, PAIRS + DENSE)

    ids = np.asarray(inputs["ids"])
    w1 = np.asarray(inputs["W_top1"])
    b1, b2, w3 = (np.asarray(inputs[n]) for n in ("b_top1", "b_top2", "W_top3"))

    arrays = {
        "ids": np.concatenate([ids[b0:b0 + n, PLACES[:ng]] for (b0, n), ng in zip(TILES, N_GATHERED)], axis=1),
        "found_ids": np.ascontiguousarray(ids[:, [f for f, _ in FOUND]].T),
        **{f"tbl_{f}": np.asarray(inputs[f"tbl_{f}"]) for f in range(F)},
        "w1": np.ascontiguousarray(w1[order]),
        "w2": np.asarray(inputs["W_top2"]),
        "small": np.concatenate([x.reshape(-1, P).T for x in (b1, b2, w3)], axis=1),
        "denseT": np.ascontiguousarray(np.asarray(inputs["dense_ctx"]).T),
    }
    nc = bacc.Bacc("TRN2", target_bir_lowering=False, num_devices=1)
    at = {n: nc.dram_tensor(n, a.shape, mybir.dt.from_np(a.dtype), kind="ExternalInput").ap()
          for n, a in arrays.items()}
    out = nc.dram_tensor("y", (1, B), F32, kind="ExternalOutput").ap()
    build(nc, at["ids"], at["found_ids"], [at[f"tbl_{f}"] for f in range(F)],
          at["w1"], at["w2"], at["small"], at["denseT"], out)
    result = run_bass_kernel_spmd(nc, [arrays], core_ids=[0])
    return result.results[0]["y"].reshape(B, 1)
```
